# Optimizing a Trainium2 kernel written in Bass

```python
import numpy as np
import jax
import jax.numpy as jnp

def _softmax(x, axis=-1):
    return jax.nn.softmax(x, axis=axis)

def _gelu(x):
    return jax.nn.gelu(x, approximate=True)

def _silu(x):
    return jax.nn.silu(x)

def _sigmoid(x):
    return jax.nn.sigmoid(x)

def _layernorm(x, axis=-1, eps=1e-05):
    m = jnp.mean(x, axis=axis, keepdims=True)
    v = jnp.var(x, axis=axis, keepdims=True)
    return (x - m) / jnp.sqrt(v + eps)

def _scatter_add(tgt, idx, src, axis=0):
    return tgt.at[idx].add(src)

def _segment_sum(src, seg, n):
    return jax.ops.segment_sum(src, seg, n)
kernel_name = 'mk_rec_standalone_d1_rec_r8_3bae86'

def setup_inputs(seed: int=0):
    np.random.seed(seed)
    _w = jnp.asarray

    def _rec_inputs():
        import jax
        import jax.numpy as jnp
        _rk = jax.random.key(seed)
        r_dense_features = -0.00338568 + 1.0005 * jax.random.normal(jax.random.fold_in(_rk, 1), (2048, 13), jnp.float32)
        r_sparse_features = jnp.stack([jax.random.randint(jax.random.fold_in(jax.random.fold_in(_rk, 2), 0), (2048,), 2, 12500, jnp.int32), jax.random.randint(jax.random.fold_in(jax.random.fold_in(_rk, 2), 1), (2048,), 1, 99999, jnp.int32), jax.random.randint(jax.random.fold_in(jax.random.fold_in(_rk, 2), 2), (2048,), 0, 12500, jnp.int32), jax.random.randint(jax.random.fold_in(jax.random.fold_in(_rk, 2), 3), (2048,), 5, 12500, jnp.int32), jax.random.randint(jax.random.fold_in(jax.random.fold_in(_rk, 2), 4), (2048,), 20, 99993, jnp.int32), jax.random.randint(jax.random.fold_in(jax.random.fold_in(_rk, 2), 5), (2048,), 0, 99993, jnp.int32), jax.random.randint(jax.random.fold_in(jax.random.fold_in(_rk, 2), 6), (2048,), 2, 99999, jnp.int32), jax.random.randint(jax.random.fold_in(jax.random.fold_in(_rk, 2), 7), (2048,), 2, 99995, jnp.int32), jax.random.randint(jax.random.fold_in(jax.random.fold_in(_rk, 2), 8), (2048,), 0, 99999, jnp.int32), jax.random.randint(jax.random.fold_in(jax.random.fold_in(_rk, 2), 9), (2048,), 2, 99986, jnp.int32), jax.random.randint(jax.random.fold_in(jax.random.fold_in(_rk, 2), 10), (2048,), 4, 99999, jnp.int32), jax.random.randint(jax.random.fold_in(jax.random.fold_in(_rk, 2), 11), (2048,), 15, 99999, jnp.int32), jax.random.randint(jax.random.fold_in(jax.random.fold_in(_rk, 2), 12), (2048,), 0, 99989, jnp.int32), jax.random.randint(jax.random.fold_in(jax.random.fold_in(_rk, 2), 13), (2048,), 5, 99990, jnp.int32), jax.random.randint(jax.random.fold_in(jax.random.fold_in(_rk, 2), 14), (2048,), 2, 99996, jnp.int32), jax.random.randint(jax.random.fold_in(jax.random.fold_in(_rk, 2), 15), (2048,), 3, 99994, jnp.int32), jax.random.randint(jax.random.fold_in(jax.random.fold_in(_rk, 2), 16), (2048,), 0, 99998, jnp.int32), jax.random.randint(jax.random.fold_in(jax.random.fold_in(_rk, 2), 17), (2048,), 13, 99998, jnp.int32), jax.random.randint(jax.random.fold_in(jax.random.fold_in(_rk, 2), 18), (2048,), 10, 12498, jnp.int32), jax.random.randint(jax.random.fold_in(jax.random.fold_in(_rk, 2), 19), (2048,), 0, 99999, jnp.int32), jax.random.randint(jax.random.fold_in(jax.random.fold_in(_rk, 2), 20), (2048,), 0, 99995, jnp.int32), jax.random.randint(jax.random.fold_in(jax.random.fold_in(_rk, 2), 21), (2048,), 1, 99998, jnp.int32), jax.random.randint(jax.random.fold_in(jax.random.fold_in(_rk, 2), 22), (2048,), 1, 99997, jnp.int32), jax.random.randint(jax.random.fold_in(jax.random.fold_in(_rk, 2), 23), (2048,), 2, 99989, jnp.int32), jax.random.randint(jax.random.fold_in(jax.random.fold_in(_rk, 2), 24), (2048,), 6, 12500, jnp.int32), jax.random.randint(jax.random.fold_in(jax.random.fold_in(_rk, 2), 25), (2048,), 2, 99995, jnp.int32)], axis=1)
        return (r_dense_features, r_sparse_features)
    r_dense_features, r_sparse_features = _rec_inputs()

    def _L0_rec_setup():
        import jax, jax.numpy as jnp
        import numpy as np
        B = 2048
        NUM_DENSE = 13
        NUM_SPARSE = 26
        VOCAB = 12500
        EMB = 64
        MLP_DIMS = [512, 256, 64]
        TOP_OUT = 256
        TRIU_I, TRIU_J = np.triu_indices(NUM_SPARSE, k=1)
        key = jax.random.key(seed)
        ks = jax.random.split(key, 12)
        inp = {}
        inp['dense_features'] = jax.random.normal(ks[0], (B, NUM_DENSE), dtype=jnp.float32)
        inp['sparse_features'] = jax.random.randint(ks[1], (B, NUM_SPARSE), 0, VOCAB, dtype=jnp.int64)
        inp['tables'] = jax.random.normal(ks[2], (NUM_SPARSE, VOCAB, EMB), dtype=jnp.float32) * 0.01
        dims = [NUM_DENSE] + MLP_DIMS
        for li in range(3):
            fan_in = dims[li]
            inp[f'W{li}'] = jax.random.normal(ks[3 + li], (dims[li], dims[li + 1]), dtype=jnp.float32) / np.sqrt(fan_in)
            inp[f'b{li}'] = jnp.zeros((dims[li + 1],), dtype=jnp.float32)
        top_in = MLP_DIMS[-1] + NUM_SPARSE * (NUM_SPARSE - 1) // 2
        inp['Wt'] = jax.random.normal(ks[6], (top_in, TOP_OUT), dtype=jnp.float32) / np.sqrt(top_in)
        inp['bt'] = jnp.zeros((TOP_OUT,), dtype=jnp.float32)
        return inp
    _L0_rec_all = _L0_rec_setup()
    _L0_rec_in = {k: v for k, v in _L0_rec_all.items() if k in ('tables', 'W0', 'b0', 'W1', 'b1', 'W2', 'b2', 'Wt', 'bt')}
    del _L0_rec_all
    return {'r_dense_features': r_dense_features, 'r_sparse_features': r_sparse_features, 'L0_rec_tables': _L0_rec_in['tables'], 'L0_rec_W0': _L0_rec_in['W0'], 'L0_rec_b0': _L0_rec_in['b0'], 'L0_rec_W1': _L0_rec_in['W1'], 'L0_rec_b1': _L0_rec_in['b1'], 'L0_rec_W2': _L0_rec_in['W2'], 'L0_rec_b2': _L0_rec_in['b2'], 'L0_rec_Wt': _L0_rec_in['Wt'], 'L0_rec_bt': _L0_rec_in['bt']}

def reference(r_dense_features, r_sparse_features, L0_rec_tables, L0_rec_W0, L0_rec_b0, L0_rec_W1, L0_rec_b1, L0_rec_W2, L0_rec_b2, L0_rec_Wt, L0_rec_bt):
    import jax
    import jax.numpy as jnp

    def _L0_rec_ref(dense_features, sparse_features, tables, W0, b0, W1, b1, W2, b2, Wt, bt):
        import jax, jax.numpy as jnp
        import numpy as np
        B = 2048
        NUM_DENSE = 13
        NUM_SPARSE = 26
        VOCAB = 12500
        EMB = 64
        MLP_DIMS = [512, 256, 64]
        TOP_OUT = 256
        TRIU_I, TRIU_J = np.triu_indices(NUM_SPARSE, k=1)
        x = jax.nn.relu(dense_features @ W0 + b0)
        x = jax.nn.relu(x @ W1 + b1)
        dense_out = jax.nn.relu(x @ W2 + b2)
        emb = jax.vmap(lambda t, idx: t[idx], in_axes=(0, 1), out_axes=1)(tables, sparse_features)
        gram = jnp.einsum('bid,bjd->bij', emb, emb)
        interact = gram[:, TRIU_I, TRIU_J]
        features = jnp.concatenate([dense_out, interact], axis=1)
        return features @ Wt + bt
    y = _L0_rec_ref(r_dense_features, r_sparse_features, L0_rec_tables, L0_rec_W0, L0_rec_b0, L0_rec_W1, L0_rec_b1, L0_rec_W2, L0_rec_b2, L0_rec_Wt, L0_rec_bt)
    return y

_drawn_inputs = setup_inputs


def setup_inputs(seed=0):
    import zlib

    import numpy as np

    out = dict(_drawn_inputs(seed))
    spreads = {'L0_rec_b0': (0.0, 0.1),
     'L0_rec_b1': (0.0, 0.1),
     'L0_rec_b2': (0.0, 0.1),
     'L0_rec_bt': (0.0, 0.1)}
    factors = {'L0_rec_tables': 8.0}
    for name, (base, spread) in spreads.items():
        noise = np.random.default_rng([zlib.crc32(name.encode()), seed]).standard_normal(out[name].shape)
        drawn = base * np.exp(spread * noise) if base else spread * noise
        out[name] = jnp.asarray(drawn.astype(out[name].dtype))
    for name, factor in factors.items():
        out[name] = (out[name] * factor).astype(out[name].dtype)
    return out
```

```python
import concourse.bass as bass
from concourse import mybir
from contextlib import ExitStack


def bass_dlrm_forward(
    nc: bass.Bass,
    dense: bass.AP,
    sparse: bass.AP,
    tables: bass.AP,
    w0: bass.AP,
    b0: bass.AP,
    w1: bass.AP,
    b1: bass.AP,
    w2: bass.AP,
    b2: bass.AP,
    wt: bass.AP,
    bt: bass.AP,
    out: bass.AP,
):
    fp32 = mybir.dt.float32
    i32 = mybir.dt.int32
    u32 = mybir.dt.uint32
    ALU = mybir.AluOpType
    ACT = mybir.ActivationFunctionType

    P = 128
    B, ND = dense.shape
    F = sparse.shape[1]
    VOCAB, EMB = tables.shape[1], tables.shape[2]
    H0, H1, H2 = w0.shape[1], w1.shape[1], w2.shape[1]
    NO = wt.shape[1]

    US = 64
    NU = B // US
    NK = F // 2
    UR = 4
    ROUNDS = NU // UR
    RS = UR * US
    CHUNKS = [range(0, 8), range(8, 12), range(12, NK)]
    FP = 32
    SQ = P // FP
    NG = US // SQ
    NJ = F - 1
    COLS = [(1, 7), (8, 6), (14, 6), (20, 6)]
    NS = max(n for _, n in COLS)
    assert sum(n for _, n in COLS) == NJ and H2 == EMB

    sparse_v = sparse.rearrange("(s u) f -> s u f", u=NU)
    out_v = out.rearrange("(s u) o -> s u o", u=NU)
    XT = B // P
    dense_v = dense.rearrange("(p t) d -> p t d", t=XT)
    tables_v = tables.rearrange("f v e -> (f v) e")

    ctx = ExitStack()
    with ctx:
        def sb(name, shape, dt=fp32):
            return ctx.enter_context(nc.sbuf_tensor(name, shape, dt))

        def pb(name, shape, dt=fp32):
            return ctx.enter_context(nc.psum_tensor(name, shape, dt))

        def sem(name):
            return ctx.enter_context(nc.semaphore(name))

        ident = sb("ident", [P, P])
        raw_idx = sb("raw_idx", [P, NU, F], i32)
        wrap = sb("wrap", [P, NU, NK])
        wrapped = sb("wrapped", [P, NU, NK])
        field_base = sb("field_base", [P, 1, NK], i32)
        later_idx = sb("later_idx", [P, NU, NK], u32)
        row_idx = sb("row_idx", [P, UR, NK], u32)
        emb = sb("emb", [P, UR, NK, EMB])
        embT = sb("embT", [EMB, 2, US, FP])
        gram = sb("gram", [P, 2, NS, P])
        x_sb = sb("x_sb", [P, XT, ND])
        xT = sb("xT", [ND, NU, US])
        w0_sb = sb("w0_sb", [ND, H0])
        w1_sb = sb("w1_sb", [P, H0 // P, H1])
        w2_sb = sb("w2_sb", [P, H1 // P, H2])
        b0_sb = sb("b0_sb", [P, H0 // P])
        b1_sb = sb("b1_sb", [P, H1 // P])
        b2_sb = sb("b2_sb", [H2, 1])
        wd_sb = sb("wd_sb", [H2 + 1, NO])
        w_tri = sb("w_tri", [FP, NJ, NO])
        w_gram = sb("w_gram", [P, NS, NO])
        h0 = sb("h0", [P, H0 // P, RS])
        h1 = sb("h1", [P, H1 // P, RS])
        h2 = sb("h2", [H2 + 1, RS])
        out_sb = sb("out_sb", [P, 2, NO])

        embT_ps = pb("embT_ps", [P, 8, 2, US])
        gram_ps = pb("gram_ps", [P, NG, P])
        mlp_ps = [pb(f"mlp_ps{i}", [P, 512]) for i in range(2)]

        zeros_set = sem("zeros_set")
        ident_ready = sem("ident_ready")
        base_ready = sem("base_ready")
        idx_in = [sem("idx_in_first"), sem("idx_in_rest")]
        idx_step = sem("idx_step")
        idx_ready = sem("idx_ready")
        later_ready = sem("later_ready")
        idx_staged = [sem(f"idx_staged_{j}") for j in range(UR)]
        tri_zeroed = sem("tri_zeroed")
        consts_set = sem("consts_set")
        x_in = sem("x_in")
        xT_in_psum = sem("xT_in_psum")
        xT_ready = sem("xT_ready")
        mlp_w_in = sem("mlp_w_in")
        tri_in = sem("tri_in")
        w_top_in = sem("w_top_in")
        rows_in = [[sem(f"rows_in_{j}_{c}") for c in range(len(CHUNKS))] for j in range(UR)]
        slot_read = [sem(f"slot_read_{j}") for j in range(UR)]
        chunk_in_psum = [sem(f"chunk_in_psum_{c}") for c in range(len(CHUNKS) - 1)]
        chunk_evac = [sem(f"chunk_evac_{c}") for c in range(len(CHUNKS))]
        gram_in_psum = [sem(f"gram_in_psum_{i}") for i in range(2)]
        gram_evac_dve = sem("gram_evac_dve")
        gram_evac_act = sem("gram_evac_act")
        l0_in_psum = sem("l0_in_psum")
        l1_in_psum = sem("l1_in_psum")
        l2_in_psum = sem("l2_in_psum")
        h0_ready = sem("h0_ready")
        h1_ready = sem("h1_ready")
        h2_ready = sem("h2_ready")
        top_in_psum = [sem(f"top_in_psum_{q}") for q in range(2)]
        out_ready = [sem(f"out_ready_{q}") for q in range(2)]
        stored = [sem(f"stored_{q}") for q in range(2)]

        PARTS = [(0, UR), (UR, NU)]
        TRI_DMAS = NJ

        def tri_row(i):
            return H2 + i * (F - 1) - i * (i - 1) // 2

        def gram_evac(copy, quads, j):
            q, half = j // 2, j % 2
            for s in quads:
                for g, (j0, n) in enumerate(COLS):
                    c0 = half * US + s
                    last = copy(
                        gram[FP * g:FP * (g + 1), q, 0:n, c0:c0 + SQ * (NG - 1) + 1:SQ],
                        gram_ps[FP * s:FP * (s + 1), :, s * NJ + j0 - 1:s * NJ + j0 - 1 + n].rearrange(
                            "p a j -> p j a"))
            return last

        def wait_from_second(eng, semaphore, count):
            if not isinstance(count, int) or count > 0:
                eng.wait_ge(semaphore, count)

        block = ctx.enter_context(nc.Block())

        @block.sync
        def _(sp):
            for part, (u0, u1) in enumerate(PARTS):
                for h in range(2):
                    sp.dma_start(raw_idx[h * US:(h + 1) * US, u0:u1, :], sparse_v[:, u0:u1, :]).then_inc(
                        idx_in[part], 16)
            sp.dma_start(w1_sb[:, :, :], w1.rearrange("(c p) n -> p c n", p=P)).then_inc(mlp_w_in, 16)
            sp.dma_start(w2_sb[:, :, :], w2.rearrange("(c p) n -> p c n", p=P)).then_inc(mlp_w_in, 16)
            sp.dma_start(wd_sb[0:H2, :], wt[0:H2, :]).then_inc(w_top_in, 16)
            sp.dma_start(wd_sb[H2:H2 + 1, :], bt.rearrange("(a n) -> a n", a=1)).then_inc(w_top_in, 16)
            sp.wait_ge(tri_zeroed, 1)
            for i in range(NJ):
                n = NJ - i
                sp.dma_start(w_tri[i:i + 1, i:NJ, :],
                             wt[tri_row(i):tri_row(i) + n, :].rearrange("(a j) n -> a j n", a=1)).then_inc(tri_in, 16)
            sp.wait_ge(tri_in, 16 * TRI_DMAS)
            for g, (j0, n) in enumerate(COLS):
                sp.dma_start(w_gram[FP * g:FP * (g + 1), 0:n, :], w_tri[:, j0 - 1:j0 - 1 + n, :]).then_inc(w_top_in, 16)
            with sp.Fori(0, ROUNDS) as r:
                for q in range(2):
                    sp.wait_ge(out_ready[q], r + 1)
                    for half in range(2):
                        u = r * UR + 2 * q + half
                        sp.dma_start(out_v[:, bass.ds(u, 1), :],
                                     out_sb[half * US:(half + 1) * US, q:q + 1, :]).then_inc(stored[q], 16)
            for q in range(2):
                sp.wait_ge(stored[q], 32 * ROUNDS)

        @block.gpsimd
        def _(pool):
            for h in range(2):
                nc.gpsimd.iota(field_base[h * US:(h + 1) * US, 0, :], pattern=[[VOCAB, NK]],
                               base=h * NK * VOCAB, channel_multiplier=0).then_inc(base_ready, 1)
            pool.wait_ge(base_ready, 2)
            pool.wait_ge(zeros_set, 1)
            nc.gpsimd.affine_select(out=ident[:, :], in_=ident[:, :], pattern=[[-1, P]], base=0,
                                    channel_multiplier=1, compare_op=ALU.not_equal, fill=1.0).then_inc(ident_ready, 1)

            def gather(r, j):
                wait_from_second(pool, slot_read[j], r)
                wait_from_second(pool, idx_staged[j], r)
                nc.gpsimd.nop(nofuse=True)
                for c, ks in enumerate(CHUNKS):
                    for k in ks:
                        nc.gpsimd.indirect_dma_start(
                            emb[:, j, k, :], None, tables_v[:, :],
                            bass.IndirectOffsetOnAxis(ap=row_idx[:, j, k:k + 1], axis=0),
                        ).then_inc(rows_in[j][c], 16)

            pool.wait_ge(idx_ready, 1)
            for j in range(UR):
                gather(0, j)
            with pool.Fori(1, ROUNDS) as r:
                for j in range(UR):
                    gather(r, j)

        @block.vector
        def _(dve):
            nc.vector.memset(ident[:, :], 0.0).then_inc(zeros_set, 1)
            steps = [0]
            for part, (u0, u1) in enumerate(PARTS):
                dve.wait_ge(idx_in[part], 32)
                halves = [(slice(h * US, (h + 1) * US), slice(h * NK, (h + 1) * NK)) for h in range(2)]
                for rows, cols in halves:
                    last = nc.vector.tensor_scalar(wrap[rows, u0:u1, :], raw_idx[rows, u0:u1, cols],
                                                   0.0, float(VOCAB), ALU.is_lt, ALU.mult)
                last.then_inc(idx_step, 1)
                dve.wait_ge(idx_step, 2 * part + 1)
                for rows, cols in halves:
                    last = nc.vector.scalar_tensor_tensor(
                        out=wrapped[rows, u0:u1, :], in0=raw_idx[rows, u0:u1, cols], scalar=float(VOCAB - 1),
                        in1=wrap[rows, u0:u1, :], op0=ALU.min, op1=ALU.add)
                last.then_inc(idx_step, 1)
                dve.wait_ge(idx_step, 2 * part + 2)
                if part == 0:
                    dve.wait_ge(base_ready, 2)
                dst = row_idx[:, :, :] if part == 0 else later_idx[:, 0:NU - UR, :]
                nc.vector.scalar_tensor_tensor(
                    out=dst, in0=wrapped[:, u0:u1, :], scalar=0.0,
                    in1=field_base[:, :, :].to_broadcast([P, u1 - u0, NK]), op0=ALU.max,
                    op1=ALU.add).then_inc(idx_ready if part == 0 else later_ready, 1)
            nc.vector.memset(embT[:, :, :, F:FP], 0.0)
            nc.vector.memset(gram[:, :, NS - 1, :], 0.0)
            nc.vector.memset(later_idx[:, NU - UR:NU, :], 0)
            nc.vector.memset(h2[H2:H2 + 1, :], 1.0).then_inc(consts_set, 1)
            nc.vector.memset(w_tri[:, :, :], 0.0)
            nc.vector.memset(w_gram[:, NS - 1, :], 0.0).then_inc(tri_zeroed, 1)
            dve.wait_ge(consts_set, 1)
            dve.wait_ge(later_ready, 1)

            def embT_evac(r, j):
                n = r * UR + j
                wait_from_second(dve, gram_in_psum[j % 2], r * 2 + j // 2)
                dst = embT[:, j % 2, :, 0:F].rearrange("p s (h k) -> p k h s", h=2)
                for c, ks in enumerate(CHUNKS):
                    if c < len(CHUNKS) - 1:
                        dve.wait_ge(chunk_in_psum[c], n + 1)
                    else:
                        dve.wait_ge(slot_read[j], r + 1)
                    t0, t1 = ks.start // 2, (ks.stop + 1) // 2
                    for odd in range(min(2, len(ks))):
                        last = nc.vector.tensor_copy(dst[:, ks.start + odd:ks.stop:2],
                                                     embT_ps[odd * EMB:(odd + 1) * EMB, t0:t1])
                    last.then_inc(chunk_evac[c], 1)

            def stage_idx(r, j):
                nc.vector.tensor_copy(row_idx[:, j:j + 1, :],
                                      later_idx[:, bass.ds(r * UR + j, 1), :]).then_inc(idx_staged[j], 1)

            def gram_half(r, j):
                dve.wait_ge(gram_in_psum[j % 2], r * 2 + j // 2 + 1)
                if j % 2 == 0:
                    wait_from_second(dve, top_in_psum[j // 2], r)
                gram_evac(nc.vector.tensor_copy, range(0, 2), j).then_inc(gram_evac_dve, 1)

            def out_evac(r, q):
                dve.wait_ge(top_in_psum[q], r + 1)
                wait_from_second(dve, stored[q], r * 32)
                nc.vector.tensor_copy(out_sb[:, q, :], mlp_ps[q][:, 0:NO]).then_inc(out_ready[q], 1)

            def vector_round(r):
                embT_evac(r, 0)
                stage_idx(r, 0)
                gram_half(r, 0)
                embT_evac(r, 1)
                stage_idx(r, 1)
                gram_half(r, 1)
                embT_evac(r, 2)
                stage_idx(r, 2)
                out_evac(r, 0)
                gram_half(r, 2)
                embT_evac(r, 3)
                stage_idx(r, 3)
                gram_half(r, 3)
                out_evac(r, 1)

            vector_round(0)
            with dve.Fori(1, ROUNDS) as r:
                vector_round(r)

        @block.scalar
        def _(act):
            act.dma_start(x_sb[:, :, :], dense_v).then_inc(x_in, 16)
            act.dma_start(w0_sb[:, :], w0).then_inc(mlp_w_in, 16)
            with nc.allow_non_contiguous_dma(reason="bias columns"):
                act.dma_start(b0_sb[:, :], b0.rearrange("(c p) -> p c", p=P)).then_inc(mlp_w_in, 16)
                act.dma_start(b1_sb[:, :], b1.rearrange("(c p) -> p c", p=P)).then_inc(mlp_w_in, 16)
                act.dma_start(b2_sb[:, :], b2.rearrange("(p c) -> p c", c=1)).then_inc(mlp_w_in, 16)
            act.wait_ge(xT_in_psum, 1)
            nc.scalar.copy(xT[:, :, :].rearrange("d (h t) s -> d t s h", h=2),
                           gram_ps[0:ND, :, :].rearrange("d t (s h) -> d t s h", h=2)).then_inc(xT_ready, 1)
            act.wait_ge(mlp_w_in, 96)

            def gram_half(r, j):
                act.wait_ge(gram_in_psum[j % 2], r * 2 + j // 2 + 1)
                if j % 2 == 0:
                    wait_from_second(act, top_in_psum[j // 2], r)
                gram_evac(nc.scalar.copy, range(2, SQ), j).then_inc(gram_evac_act, 1)

            def scalar_round(r):
                for half in range(2):
                    act.wait_ge(l0_in_psum, r * 2 + half + 1)
                    for m in range(2):
                        c = 2 * half + m
                        last = nc.scalar.activation(h0[:, c, :], mlp_ps[half][:, m * RS:(m + 1) * RS], ACT.Relu,
                                                    bias=b0_sb[:, c:c + 1])
                last.then_inc(h0_ready, 1)
                act.wait_ge(l1_in_psum, r + 1)
                for m in range(2):
                    last = nc.scalar.activation(h1[:, m, :], mlp_ps[0][:, m * RS:(m + 1) * RS], ACT.Relu,
                                                bias=b1_sb[:, m:m + 1])
                last.then_inc(h1_ready, 1)
                gram_half(r, 0)
                act.wait_ge(l2_in_psum, r + 1)
                nc.scalar.activation(h2[0:H2, :], mlp_ps[1][0:H2, 0:RS], ACT.Relu,
                                     bias=b2_sb[:, 0:1]).then_inc(h2_ready, 1)
                for j in range(1, UR):
                    gram_half(r, j)

            scalar_round(0)
            with act.Fori(1, ROUNDS) as r:
                scalar_round(r)

        @block.tensor
        def _(pe):
            pe.wait_ge(ident_ready, 1)
            pe.wait_ge(x_in, 16)
            for t in range(XT):
                last = nc.tensor.transpose(gram_ps[0:ND, t, :], x_sb[:, t, :], ident[:, :])
            last.then_inc(xT_in_psum, 1)
            pe.wait_ge(xT_ready, 1)
            pe.wait_ge(mlp_w_in, 96)
            pe.wait_ge(consts_set, 1)

            def mlp_l0(r):
                for half in range(2):
                    wait_from_second(pe, out_ready[half], r)
                    nc.tensor.nop(nofuse=True)
                    for m in range(2):
                        c = 2 * half + m
                        last = nc.tensor.matmul(mlp_ps[half][:, m * RS:(m + 1) * RS], w0_sb[:, c * P:(c + 1) * P],
                                                xT[:, bass.ds(r * UR, UR), :], start=True, stop=True)
                    last.then_inc(l0_in_psum, 1)

            def mlp_l1(r):
                pe.wait_ge(h0_ready, r + 1)
                for m in range(2):
                    for c in range(H0 // P):
                        last = nc.tensor.matmul(mlp_ps[0][:, m * RS:(m + 1) * RS], w1_sb[:, c, m * P:(m + 1) * P],
                                                h0[:, c, :], start=(c == 0), stop=(c == H0 // P - 1))
                last.then_inc(l1_in_psum, 1)

            def mlp_l2(r):
                pe.wait_ge(h1_ready, r + 1)
                for c in range(H1 // P):
                    last = nc.tensor.matmul(mlp_ps[1][0:H2, 0:RS], w2_sb[:, c, :], h1[:, c, :],
                                            start=(c == 0), stop=(c == H1 // P - 1))
                last.then_inc(l2_in_psum, 1)

            def transposes(r, j):
                n = r * UR + j
                for c, ks in enumerate(CHUNKS):
                    pe.wait_ge(rows_in[j][c], (r + 1) * (16 * len(ks)))
                    if c == 0:
                        wait_from_second(pe, chunk_evac[0], n)
                    elif c == 1:
                        wait_from_second(pe, chunk_evac[2], n)
                    else:
                        pe.wait_ge(chunk_evac[1], n + 1)
                    if len(ks) == 1:
                        nc.tensor.nop(nofuse=True)
                    for k in ks[::2]:
                        m = min(2, ks.stop - k)
                        last = nc.tensor.transpose(embT_ps[0:m * EMB, k // 2, :, :], emb[:, j, k:k + m, :],
                                                   ident[:, :])
                    last.then_inc(slot_read[j] if c == len(CHUNKS) - 1 else chunk_in_psum[c], 1)

            def gram_products(r, j):
                n = r * UR + j
                pe.wait_ge(chunk_evac[-1], n + 1)
                wait_from_second(pe, gram_evac_dve, n)
                wait_from_second(pe, gram_evac_act, n)
                for a in range(NG):
                    last = nc.tensor.matmul(gram_ps[:, a, 0:SQ * NJ],
                                            embT[:, j % 2, a * SQ:(a + 1) * SQ, :].rearrange("p s f -> p (s f)"),
                                            embT[:, j % 2, a * SQ:(a + 1) * SQ, 1:F], start=True, stop=True)
                last.then_inc(gram_in_psum[j % 2], 1)

            def top(r, q):
                pe.wait_ge(h2_ready, r + 1)
                nc.tensor.matmul(mlp_ps[q][:, 0:NO], h2[:, q * P:(q + 1) * P], wd_sb[:, :], start=True, stop=False)
                pe.wait_ge(gram_evac_dve, r * UR + 2 * q + 2)
                pe.wait_ge(gram_evac_act, r * UR + 2 * q + 2)
                for i in range(NS):
                    last = nc.tensor.matmul(mlp_ps[q][:, 0:NO], gram[:, q, i, :], w_gram[:, i, :],
                                            start=False, stop=(i == NS - 1))
                last.then_inc(top_in_psum[q], 1)

            def tensor_round(r):
                mlp_l0(r)
                transposes(r, 0)
                mlp_l1(r)
                gram_products(r, 0)
                mlp_l2(r)
                transposes(r, 1)
                gram_products(r, 1)
                transposes(r, 2)
                pe.wait_ge(w_top_in, 96)
                pe.wait_ge(tri_zeroed, 1)
                top(r, 0)
                gram_products(r, 2)
                transposes(r, 3)
                gram_products(r, 3)
                top(r, 1)

            tensor_round(0)
            with pe.Fori(1, ROUNDS) as r:
                tensor_round(r)


_INS = ['r_dense_features', 'r_sparse_features', 'L0_rec_tables', 'L0_rec_W0', 'L0_rec_b0', 'L0_rec_W1',
        'L0_rec_b1', 'L0_rec_W2', 'L0_rec_b2', 'L0_rec_Wt', 'L0_rec_bt']
_OUTS = [((2048, 256), 'float32')]


def kernel(**inputs):
    import numpy as _np
    import concourse.bacc as _bacc
    from concourse import mybir as _mybir
    from concourse.bass_utils import run_bass_kernel_spmd as _run

    nc = _bacc.Bacc("TRN2", target_bir_lowering=False, num_devices=1)
    arrays, args = {}, []
    for name in _INS:
        a = _np.ascontiguousarray(inputs[name])
        arrays[f"in_{name}_dram"] = a
        args.append(nc.dram_tensor(f"in_{name}_dram", a.shape, _mybir.dt.from_np(a.dtype), kind="ExternalInput").ap())
    for i, (shape, dtype) in enumerate(_OUTS):
        dt = _mybir.dt.from_np(_np.dtype(dtype))
        args.append(nc.dram_tensor(f"out_{i}_dram", shape, dt, kind="ExternalOutput").ap())
    bass_dlrm_forward(nc, *args)
    r = _run(nc, [arrays], core_ids=[0])
    got = tuple(r.results[0][f"out_{i}_dram"] for i in range(len(_OUTS)))
    return got[0]
```

```python
import concourse.bass as bass
from concourse import mybir
from contextlib import ExitStack


def bass_dlrm_forward(
    nc: bass.Bass,
    dense: bass.AP,
    sparse: bass.AP,
    tables: bass.AP,
    w0: bass.AP,
    b0: bass.AP,
    w1: bass.AP,
    b1: bass.AP,
    w2: bass.AP,
    b2: bass.AP,
    wt: bass.AP,
    bt: bass.AP,
    out: bass.AP,
):
    fp32 = mybir.dt.float32
    i32 = mybir.dt.int32
    u32 = mybir.dt.uint32
    ALU = mybir.AluOpType
    ACT = mybir.ActivationFunctionType

    P = 128
    B, ND = dense.shape
    F = sparse.shape[1]
    VOCAB, EMB = tables.shape[1], tables.shape[2]
    H0, H1, H2 = w0.shape[1], w1.shape[1], w2.shape[1]
    NO = wt.shape[1]

    US = 64
    NU = B // US
    NP = NU // 2
    UR = 4
    ROUNDS = NU // UR
    RS = UR * US
    NK = F // 2
    FP = 32
    SQ = P // FP
    NG = US // SQ
    HG = NG // 2
    NS = F // SQ + 1
    CHUNKS = [range(0, 8), range(8, 12), range(12, NK)]
    LAST = len(CHUNKS) - 1
    BANK = [0, 1, 1]
    assert all(ks.start % 2 == 0 and ks.stop <= 8 * (bank + 1) for ks, bank in zip(CHUNKS, BANK))

    def col(t, g):
        return SQ * t + g - 2

    def first_slot(g):
        return 0 if col(0, g) > 0 else 1

    sparse_v = sparse.rearrange("(h s t) f -> s h t f", h=2, t=NP)
    out_v = out.rearrange("(m t) o -> m t o", t=NP)
    dense_v = dense.rearrange("(m t) d -> m t d", t=NP)
    tables_v = tables.rearrange("f v e -> (f v) e")

    ctx = ExitStack()
    with ctx:
        def sb(name, shape, dt=fp32):
            return ctx.enter_context(nc.sbuf_tensor(name, shape, dt))

        def pb(name, shape, dt=fp32):
            return ctx.enter_context(nc.psum_tensor(name, shape, dt))

        def sem(name):
            return ctx.enter_context(nc.semaphore(name))

        ident = sb("ident", [P, P])
        raw_idx = sb("raw_idx", [P, 2, NP, F], i32)
        wrap = sb("wrap", [P, NU, NK])
        capped = sb("capped", [P, NU, NK])
        wrapped = sb("wrapped", [P, NU, NK])
        field_base = sb("field_base", [P, 1, NK], i32)
        later_idx = sb("later_idx", [P, NU, NK], u32)
        row_idx = sb("row_idx", [P, UR, NK], u32)
        emb = sb("emb", [P, UR, NK, EMB])
        embT = sb("embT", [P, 2, US, FP])
        gram = sb("gram", [P, 2, NS, P])
        x_sb = sb("x_sb", [P, NP, ND])
        xT = sb("xT", [ND, NP, P])
        w0_sb = sb("w0_sb", [ND, H0])
        w1_sb = sb("w1_sb", [P, H0 // P, H1])
        w2_sb = sb("w2_sb", [P, H1 // P, H2])
        b0_sb = sb("b0_sb", [P, H0 // P])
        b1_sb = sb("b1_sb", [P, H1 // P])
        b2_sb = sb("b2_sb", [H2, 1])
        wd_sb = sb("wd_sb", [H2 + 1, NO])
        w_tri = sb("w_tri", [FP, F - 1, NO])
        w_gram = sb("w_gram", [P, NS, NO])
        h0 = sb("h0", [P, H0 // P, RS])
        h1 = sb("h1", [P, H1 // P, RS])
        h2 = sb("h2", [H2 + 1, RS])
        out_sb = sb("out_sb", [P, 2, NO])

        rowsT_ps = [pb(f"rowsT_ps_{i}", [P, 4, 2, US]) for i in range(2)]
        gram_ps = pb("gram_ps", [P, NG, P])
        mlp_ps = [pb(f"mlp_ps{i}", [P, 512]) for i in range(2)]

        zeros_set = sem("zeros_set")
        ident_ready = sem("ident_ready")
        base_ready = sem("base_ready")
        idx_in = [sem("idx_in_first"), sem("idx_in_rest")]
        idx_step = sem("idx_step")
        idx_ready = sem("idx_ready")
        later_ready = sem("later_ready")
        idx_staged = sem("idx_staged")
        tri_zeroed = sem("tri_zeroed")
        consts_set = sem("consts_set")
        x_in = sem("x_in")
        xT_in_psum = sem("xT_in_psum")
        xT_ready = sem("xT_ready")
        mlp_w_in = sem("mlp_w_in")
        tri_in = sem("tri_in")
        w_top_in = sem("w_top_in")
        rows_in = [[sem(f"rows_in_{j}_{c}") for c in range(len(CHUNKS))] for j in range(UR)]
        rowsT_in_psum = [sem(f"rowsT_in_psum_{c}") for c in range(len(CHUNKS))]
        embT_even = [sem(f"embT_even_{c}") for c in range(len(CHUNKS))]
        embT_odd = [sem(f"embT_odd_{c}") for c in range(len(CHUNKS))]
        gram_in_psum = sem("gram_in_psum")
        gram_evac_dve = sem("gram_evac_dve")
        gram_evac_act = sem("gram_evac_act")
        l0_in_psum = sem("l0_in_psum")
        l1_in_psum = sem("l1_in_psum")
        l2_in_psum = sem("l2_in_psum")
        h0_ready = sem("h0_ready")
        h1_ready = sem("h1_ready")
        h2_ready = sem("h2_ready")
        top_in_psum = [sem(f"top_in_psum_{q}") for q in range(2)]
        out_ready = [sem(f"out_ready_{q}") for q in range(2)]
        stored = [sem(f"stored_{q}") for q in range(2)]

        PARTS = [(0, UR), (UR, NU)]

        def tri_row(i):
            return H2 + i * (F - 1) - i * (i - 1) // 2

        def rowsT_evac(copy, c, odd, j):
            ks = CHUNKS[c]
            i = (ks.start - 8 * BANK[c]) // 2
            m = len(ks[odd::2])
            dst = embT[0:EMB, j % 2, :, 0:F].rearrange("p s (k x) -> p k x s", x=2)
            return copy(dst[:, ks.start + odd:ks.stop:2],
                        rowsT_ps[BANK[c]][odd * EMB:(odd + 1) * EMB, i:i + m])

        BLOCKS = [(s, g) for s in range(SQ) for g in range(SQ)]
        DVE_BLOCKS, ACT_BLOCKS = BLOCKS[:len(BLOCKS) // 2], BLOCKS[len(BLOCKS) // 2:]

        def gram_evac(copy, blocks, j, half):
            q, c0, a0, a1 = j // 2, (j % 2) * US, half * HG, (half + 1) * HG
            for s, g in blocks:
                t0 = first_slot(g)
                src = s * (F - 1) + col(t0, g) - 1
                last = copy(
                    gram[FP * g:FP * (g + 1), q, t0:NS, c0 + a0 * SQ + s:c0 + a1 * SQ:SQ],
                    gram_ps[FP * s:FP * (s + 1), a0:a1, src:src + SQ * (NS - t0 - 1) + 1:SQ].rearrange("p a t -> p t a"))
            return last

        def wait_if_any(eng, semaphore, count):
            if not isinstance(count, int) or count > 0:
                eng.wait_ge(semaphore, count)

        block = ctx.enter_context(nc.Block())

        @block.sync
        def _(sp):
            sp.dma_start(raw_idx[0:US, :, 0:UR // 2, :], sparse_v[:, :, 0:UR // 2, :]).then_inc(idx_in[0], 16)
            for x in range(2):
                sp.dma_start(raw_idx[x * US:(x + 1) * US, :, UR // 2:NP, :], sparse_v[:, :, UR // 2:NP, :]).then_inc(
                    idx_in[1], 16)
            sp.dma_start(w1_sb[:, :, :], w1.rearrange("(c p) n -> p c n", p=P)).then_inc(mlp_w_in, 16)
            sp.dma_start(w2_sb[:, :, :], w2.rearrange("(c p) n -> p c n", p=P)).then_inc(mlp_w_in, 16)
            sp.dma_start(wd_sb[0:H2, :], wt[0:H2, :]).then_inc(w_top_in, 16)
            sp.dma_start(wd_sb[H2:H2 + 1, :], bt.rearrange("(a n) -> a n", a=1)).then_inc(w_top_in, 16)
            sp.wait_ge(tri_zeroed, 1)
            for i in range(F - 1):
                n = F - 1 - i
                sp.dma_start(w_tri[i:i + 1, i:F - 1, :],
                             wt[tri_row(i):tri_row(i) + n, :].rearrange("(a j) n -> a j n", a=1)).then_inc(tri_in, 16)
            sp.wait_ge(tri_in, 16 * (F - 1))
            for g in range(SQ):
                t0 = first_slot(g)
                sp.dma_start(w_gram[FP * g:FP * (g + 1), t0:NS, :],
                             w_tri[:, col(t0, g) - 1:F - 1:SQ, :]).then_inc(w_top_in, 16)
            with sp.Fori(0, ROUNDS) as r:
                for q in range(2):
                    sp.wait_ge(out_ready[q], r + 1)
                    sp.dma_start(out_v[:, bass.ds(r * 2 + q, 1), :], out_sb[:, q:q + 1, :]).then_inc(stored[q], 16)
            for q in range(2):
                sp.wait_ge(stored[q], 16 * ROUNDS)

        @block.gpsimd
        def _(pool):
            for x in range(2):
                nc.gpsimd.iota(field_base[x * US:(x + 1) * US, 0, :], pattern=[[2 * VOCAB, NK]],
                               base=x * VOCAB, channel_multiplier=0).then_inc(base_ready, 1)
            pool.wait_ge(base_ready, 2)
            pool.wait_ge(zeros_set, 1)
            nc.gpsimd.affine_select(out=ident[:, :], in_=ident[:, :], pattern=[[-1, P]], base=0,
                                    channel_multiplier=1, compare_op=ALU.not_equal, fill=1.0).then_inc(ident_ready, 1)

            def gather(r, j):
                wait_if_any(pool, rowsT_in_psum[LAST], r * UR + j + 1 - UR)
                wait_if_any(pool, idx_staged, r * UR + j + 1 - UR)
                nc.gpsimd.nop(nofuse=True)
                for c, ks in enumerate(CHUNKS):
                    for k in ks:
                        nc.gpsimd.indirect_dma_start(
                            emb[:, j, k, :], None, tables_v[:, :],
                            bass.IndirectOffsetOnAxis(ap=row_idx[:, j, k:k + 1], axis=0),
                        ).then_inc(rows_in[j][c], 16)

            pool.wait_ge(idx_ready, 1)
            for j in range(UR):
                gather(0, j)
            with pool.Fori(1, ROUNDS) as r:
                for j in range(UR):
                    gather(r, j)

        @block.vector
        def _(dve):
            nc.vector.memset(ident[:, :], 0.0).then_inc(zeros_set, 1)
            for part, (u0, u1) in enumerate(PARTS):
                dve.wait_ge(idx_in[part], 32)
                halves = [(slice(x * US, (x + 1) * US),
                           raw_idx[x * US:(x + 1) * US, :, u0 // 2:u1 // 2, x:F:2].rearrange("s h t k -> s t h k"))
                          for x in range(2)]

                def by_unit(buf, rows):
                    return buf[rows, u0:u1, :].rearrange("s (t h) k -> s t h k", h=2)

                for rows, raw in halves:
                    nc.vector.tensor_scalar(by_unit(wrap, rows), raw, 0.0, float(VOCAB), ALU.is_lt, ALU.mult)
                    last = nc.vector.tensor_scalar(by_unit(capped, rows), raw, float(VOCAB - 1), None, ALU.min)
                last.then_inc(idx_step, 1)
                dve.wait_ge(idx_step, 2 * part + 1)
                nc.vector.tensor_tensor(wrapped[:, u0:u1, :], capped[:, u0:u1, :], wrap[:, u0:u1, :],
                                        ALU.add).then_inc(idx_step, 1)
                dve.wait_ge(idx_step, 2 * part + 2)
                if part == 0:
                    dve.wait_ge(base_ready, 2)
                dst = row_idx[:, :, :] if part == 0 else later_idx[:, 0:NU - UR, :]
                nc.vector.scalar_tensor_tensor(
                    out=dst, in0=wrapped[:, u0:u1, :], scalar=0.0,
                    in1=field_base[:, :, :].to_broadcast([P, u1 - u0, NK]), op0=ALU.max,
                    op1=ALU.add).then_inc(idx_ready if part == 0 else later_ready, 1)
            nc.vector.memset(embT[:, :, :, :], 0.0)
            nc.vector.memset(gram[:, :, 0, :], 0.0)
            nc.vector.memset(later_idx[:, NU - UR:NU, :], 0)
            nc.vector.memset(h2[H2:H2 + 1, :], 1.0).then_inc(consts_set, 1)
            nc.vector.memset(w_tri[:, :, :], 0.0)
            nc.vector.memset(w_gram[:, 0, :], 0.0).then_inc(tri_zeroed, 1)
            dve.wait_ge(consts_set, 1)
            dve.wait_ge(later_ready, 1)

            def embT_evac(r, j):
                n = r * UR + j
                wait_if_any(dve, gram_in_psum, (n - 1) * 2)
                for c in range(len(CHUNKS)):
                    dve.wait_ge(rowsT_in_psum[c], n + 1)
                    rowsT_evac(nc.vector.tensor_copy, c, 0, j).then_inc(embT_even[c], 1)

            def stage_idx(r, j):
                nc.vector.tensor_copy(row_idx[:, j:j + 1, :],
                                      later_idx[:, bass.ds(r * UR + j, 1), :]).then_inc(idx_staged, 1)

            def gram_blocks(r, j):
                if j % 2 == 0:
                    wait_if_any(dve, top_in_psum[j // 2], r)
                for half in range(2):
                    dve.wait_ge(gram_in_psum, (r * UR + j) * 2 + half + 1)
                    gram_evac(nc.vector.tensor_copy, DVE_BLOCKS, j, half).then_inc(gram_evac_dve, 1)

            def out_evac(r, q):
                dve.wait_ge(top_in_psum[q], r + 1)
                wait_if_any(dve, stored[q], r * 16)
                nc.vector.tensor_copy(out_sb[:, q, :], mlp_ps[q][:, 0:NO]).then_inc(out_ready[q], 1)

            def vector_round(r, first=False):
                for j in range(UR):
                    embT_evac(r, j)
                    stage_idx(r, j)
                    if j == 0 and not first:
                        out_evac(r - 1, 1)
                    if j == 3:
                        out_evac(r, 0)
                    gram_blocks(r, j)

            vector_round(0, first=True)
            with dve.Fori(1, ROUNDS) as r:
                vector_round(r)
            out_evac(ROUNDS - 1, 1)

        @block.scalar
        def _(act):
            act.dma_start(raw_idx[US:P, :, 0:UR // 2, :], sparse_v[:, :, 0:UR // 2, :]).then_inc(idx_in[0], 16)
            act.dma_start(x_sb[:, :, :], dense_v).then_inc(x_in, 16)
            act.dma_start(w0_sb[:, :], w0).then_inc(mlp_w_in, 16)
            with nc.allow_non_contiguous_dma(reason="bias columns"):
                act.dma_start(b0_sb[:, :], b0.rearrange("(c p) -> p c", p=P)).then_inc(mlp_w_in, 16)
                act.dma_start(b1_sb[:, :], b1.rearrange("(c p) -> p c", p=P)).then_inc(mlp_w_in, 16)
                act.dma_start(b2_sb[:, :], b2.rearrange("(p c) -> p c", c=1)).then_inc(mlp_w_in, 16)
            for i in range(4):
                act.wait_ge(xT_in_psum, i + 1)
                nc.scalar.copy(xT[:, 4 * i:4 * i + 4, :], rowsT_ps[i % 2][0:ND, :, :, :]).then_inc(xT_ready, 1)
            act.wait_ge(consts_set, 1)
            act.wait_ge(mlp_w_in, 96)

            def embT_evac(r, j):
                n = r * UR + j
                wait_if_any(act, gram_in_psum, (n - 1) * 2)
                for c in range(len(CHUNKS)):
                    if len(CHUNKS[c]) > 1:
                        act.wait_ge(rowsT_in_psum[c], n + 1)
                        rowsT_evac(nc.scalar.copy, c, 1, j).then_inc(embT_odd[c], 1)

            def gram_blocks(r, j):
                if j % 2 == 0:
                    wait_if_any(act, top_in_psum[j // 2], r)
                for half in range(2):
                    act.wait_ge(gram_in_psum, (r * UR + j) * 2 + half + 1)
                    gram_evac(nc.scalar.copy, ACT_BLOCKS, j, half).then_inc(gram_evac_act, 1)

            def l0_evac(r):
                for half in range(2):
                    act.wait_ge(l0_in_psum, r * 2 + half + 1)
                    for m in range(2):
                        c = 2 * half + m
                        last = nc.scalar.activation(h0[:, c, :], mlp_ps[half][:, m * RS:(m + 1) * RS], ACT.Relu,
                                                    bias=b0_sb[:, c:c + 1])
                last.then_inc(h0_ready, 1)

            def l1_evac(r):
                act.wait_ge(l1_in_psum, r + 1)
                for m in range(2):
                    last = nc.scalar.activation(h1[:, m, :], mlp_ps[0][:, m * RS:(m + 1) * RS], ACT.Relu,
                                                bias=b1_sb[:, m:m + 1])
                last.then_inc(h1_ready, 1)

            def l2_evac(r):
                act.wait_ge(l2_in_psum, r + 1)
                nc.scalar.activation(h2[0:H2, :], mlp_ps[1][0:H2, 0:RS], ACT.Relu,
                                     bias=b2_sb[:, 0:1]).then_inc(h2_ready, 1)

            def scalar_round(r):
                embT_evac(r, 0)
                gram_blocks(r, 0)
                embT_evac(r, 1)
                l0_evac(r)
                gram_blocks(r, 1)
                l1_evac(r)
                embT_evac(r, 2)
                l2_evac(r)
                gram_blocks(r, 2)
                embT_evac(r, 3)
                gram_blocks(r, 3)

            scalar_round(0)
            with act.Fori(1, ROUNDS) as r:
                scalar_round(r)

        @block.tensor
        def _(pe):
            pe.wait_ge(ident_ready, 1)
            pe.wait_ge(x_in, 16)
            for t in range(NP):
                i, u = t // 4, t % 4
                if u == 0 and i >= 2:
                    pe.wait_ge(xT_ready, i - 1)
                last = nc.tensor.transpose(rowsT_ps[i % 2][0:ND, u, :, :], x_sb[:, t, :], ident[:, :])
                if u == 3:
                    last.then_inc(xT_in_psum, 1)
            pe.wait_ge(xT_ready, 4)
            pe.wait_ge(mlp_w_in, 96)
            pe.wait_ge(consts_set, 1)

            def mlp_l0(r):
                for half in range(2):
                    wait_if_any(pe, out_ready[half], r)
                    nc.tensor.nop(nofuse=True)
                    for m in range(2):
                        c = 2 * half + m
                        last = nc.tensor.matmul(mlp_ps[half][:, m * RS:(m + 1) * RS], w0_sb[:, c * P:(c + 1) * P],
                                                xT[:, bass.ds(r * 2, 2), :], start=True, stop=True)
                    last.then_inc(l0_in_psum, 1)

            def mlp_l1(r):
                pe.wait_ge(h0_ready, r + 1)
                for m in range(2):
                    for c in range(H0 // P):
                        last = nc.tensor.matmul(mlp_ps[0][:, m * RS:(m + 1) * RS], w1_sb[:, c, m * P:(m + 1) * P],
                                                h0[:, c, :], start=(c == 0), stop=(c == H0 // P - 1))
                last.then_inc(l1_in_psum, 1)

            def mlp_l2(r):
                pe.wait_ge(h1_ready, r + 1)
                for c in range(H1 // P):
                    last = nc.tensor.matmul(mlp_ps[1][0:H2, 0:RS], w2_sb[:, c, :], h1[:, c, :],
                                            start=(c == 0), stop=(c == H1 // P - 1))
                last.then_inc(l2_in_psum, 1)

            def transposes(r, j, chunks=range(len(CHUNKS))):
                n = r * UR + j
                for c in chunks:
                    ks = CHUNKS[c]
                    pe.wait_ge(rows_in[j][c], (r + 1) * (16 * len(ks)))
                    if c == 0:
                        wait_if_any(pe, embT_even[0], n)
                        wait_if_any(pe, embT_odd[0], n)
                    elif c == 1:
                        wait_if_any(pe, embT_even[LAST], n)
                    else:
                        pe.wait_ge(embT_even[c - 1], n + 1)
                        pe.wait_ge(embT_odd[c - 1], n + 1)
                    if len(ks) == 1:
                        nc.tensor.nop(nofuse=True)
                    for k in ks[::2]:
                        m = min(2, ks.stop - k)
                        last = nc.tensor.transpose(rowsT_ps[BANK[c]][0:m * EMB, (k - 8 * BANK[c]) // 2, :, :],
                                                   emb[:, j, k:k + m, :], ident[:, :])
                    last.then_inc(rowsT_in_psum[c], 1)

            def gram_products(r, j):
                n = r * UR + j
                pe.wait_ge(embT_even[LAST], n + 1)
                pe.wait_ge(embT_odd[LAST - 1], n + 1)
                for half in range(2):
                    wait_if_any(pe, gram_evac_dve, (n - 1) * 2 + half + 1)
                    wait_if_any(pe, gram_evac_act, (n - 1) * 2 + half + 1)
                    for a in range(half * HG, (half + 1) * HG):
                        samples = embT[:, j % 2, a * SQ:(a + 1) * SQ, :]
                        last = nc.tensor.matmul(gram_ps[:, a, 0:SQ * (F - 1)], samples.rearrange("p s f -> p (s f)"),
                                                samples[:, :, 1:F], start=True, stop=True)
                    last.then_inc(gram_in_psum, 1)

            def top(r, q, slots=range(NS)):
                if slots.start == 0:
                    pe.wait_ge(h2_ready, r + 1)
                    nc.tensor.matmul(mlp_ps[q][:, 0:NO], h2[:, q * P:(q + 1) * P], wd_sb[:, :],
                                     start=True, stop=False)
                    pe.wait_ge(gram_evac_dve, (r * UR + 2 * q + 2) * 2)
                    pe.wait_ge(gram_evac_act, (r * UR + 2 * q + 2) * 2)
                for t in slots:
                    last = nc.tensor.matmul(mlp_ps[q][:, 0:NO], gram[:, q, t, :], w_gram[:, t, :],
                                            start=False, stop=(t == NS - 1))
                if slots.stop == NS:
                    last.then_inc(top_in_psum[q], 1)

            def tensor_round(r, first=False):
                transposes(r, 0)
                if not first:
                    top(r - 1, 1)
                gram_products(r, 0)
                transposes(r, 1)
                mlp_l0(r)
                gram_products(r, 1)
                mlp_l1(r)
                transposes(r, 2)
                mlp_l2(r)
                gram_products(r, 2)
                transposes(r, 3, range(1))
                if first:
                    pe.wait_ge(w_top_in, 96)
                    pe.wait_ge(tri_zeroed, 1)
                top(r, 0, range(0, 3))
                transposes(r, 3, range(1, 2))
                top(r, 0, range(3, NS))
                transposes(r, 3, range(2, 3))
                gram_products(r, 3)

            tensor_round(0, first=True)
            with pe.Fori(1, ROUNDS) as r:
                tensor_round(r)
            top(ROUNDS - 1, 1)


_INS = ['r_dense_features', 'r_sparse_features', 'L0_rec_tables', 'L0_rec_W0', 'L0_rec_b0', 'L0_rec_W1',
        'L0_rec_b1', 'L0_rec_W2', 'L0_rec_b2', 'L0_rec_Wt', 'L0_rec_bt']
_OUTS = [((2048, 256), 'float32')]


def kernel(**inputs):
    import numpy as _np
    import concourse.bacc as _bacc
    from concourse import mybir as _mybir
    from concourse.bass_utils import run_bass_kernel_spmd as _run

    nc = _bacc.Bacc("TRN2", target_bir_lowering=False, num_devices=1)
    arrays, args = {}, []
    for name in _INS:
        a = _np.ascontiguousarray(inputs[name])
        arrays[f"in_{name}_dram"] = a
        args.append(nc.dram_tensor(f"in_{name}_dram", a.shape, _mybir.dt.from_np(a.dtype), kind="ExternalInput").ap())
    for i, (shape, dtype) in enumerate(_OUTS):
        dt = _mybir.dt.from_np(_np.dtype(dtype))
        args.append(nc.dram_tensor(f"out_{i}_dram", shape, dt, kind="ExternalOutput").ap())
    bass_dlrm_forward(nc, *args)
    r = _run(nc, [arrays], core_ids=[0])
    got = tuple(r.results[0][f"out_{i}_dram"] for i in range(len(_OUTS)))
    return got[0]
```
